# Optimizing a Trainium2 kernel written in Bass

```python
import numpy as np
import jax
import jax.numpy as jnp

def _softmax(x, axis=-1):
    return jax.nn.softmax(x, axis=axis)

def _gelu(x):
    return jax.nn.gelu(x, approximate=True)

def _silu(x):
    return jax.nn.silu(x)

def _sigmoid(x):
    return jax.nn.sigmoid(x)

def _layernorm(x, axis=-1, eps=1e-05):
    m = jnp.mean(x, axis=axis, keepdims=True)
    v = jnp.var(x, axis=axis, keepdims=True)
    return (x - m) / jnp.sqrt(v + eps)

def _scatter_add(tgt, idx, src, axis=0):
    return tgt.at[idx].add(src)

def _segment_sum(src, seg, n):
    return jax.ops.segment_sum(src, seg, n)
kernel_name = 'mk_cond_resid_d1_seqx_r2_0828ef'

def setup_inputs(seed: int=0):
    np.random.seed(seed)
    _w = jnp.asarray

    def _rec_inputs():
        import jax
        import jax.numpy as jnp
        _rk = jax.random.key(seed)
        x = 7.22e-05 + 1 * jax.random.normal(jax.random.fold_in(_rk, 1), (32, 512, 512), jnp.float32)
        _lenS = 512 - jax.random.randint(jax.random.fold_in(_rk, 7), (32,), 0, max(1, 512 // 4) + 1, jnp.int32)
        _lenS2 = 512 - jax.random.randint(jax.random.fold_in(_rk, 8), (32,), 0, max(1, 512 // 4) + 1, jnp.int32)
        fside_BxSxS_0 = 4.13588e-05 + 0.999923 * jax.random.normal(jax.random.fold_in(_rk, 11), (32, 512, 512), jnp.float32)
        itok_B_0_5 = jax.random.randint(jax.random.fold_in(_rk, 12), (32,), 0, 6, jnp.int32)
        return (x, fside_BxSxS_0, itok_B_0_5)
    x, fside_BxSxS_0, itok_B_0_5 = _rec_inputs()

    def _L0_cond_setup():
        import jax, jax.numpy as jnp
        import numpy as np
        B, S, D = (8, 512, 512)
        NUM_STAGES = 6
        key = jax.random.key(seed)
        k1, k2, k3, k4, k5 = jax.random.split(key, 5)
        return {'query': jax.random.normal(k1, (B, S, D), dtype=jnp.float32), 'key': jax.random.normal(k2, (B, S, D), dtype=jnp.float32), 'value': jax.random.normal(k3, (B, S, D), dtype=jnp.float32), 'braak_embed': jax.random.normal(k4, (NUM_STAGES, D), dtype=jnp.float32), 'braak_stages': jax.random.randint(k5, (B,), 0, NUM_STAGES, dtype=jnp.int64)}
    _L0_cond_all = _L0_cond_setup()
    _L0_cond_in = {k: v for k, v in _L0_cond_all.items() if k in ('braak_embed',)}
    del _L0_cond_all
    return {'x': x, 'fside_BxSxS_0': fside_BxSxS_0, 'itok_B_0_5': itok_B_0_5, 'L0_cond_braak_embed': _L0_cond_in['braak_embed']}

def reference(x, fside_BxSxS_0, itok_B_0_5, L0_cond_braak_embed):
    import jax
    import jax.numpy as jnp

    def _L0_cond_ref(query, key, value, braak_embed, braak_stages):
        import jax, jax.numpy as jnp
        import numpy as np
        B, S, D = (8, 512, 512)
        NUM_STAGES = 6
        bias = braak_embed[braak_stages][..., None]
        q = query + bias
        attn = jnp.einsum('bsd,btd->bst', q, key)
        attn = jax.nn.softmax(attn, axis=-1)
        return jnp.einsum('bst,btd->bsd', attn, value)
    x = x + _L0_cond_ref(x, fside_BxSxS_0, fside_BxSxS_0, L0_cond_braak_embed, itok_B_0_5)
    return x

_drawn_inputs = setup_inputs


def setup_inputs(seed=0):
    import zlib

    import numpy as np

    out = dict(_drawn_inputs(seed))
    spreads = {}
    factors = {}
    for name, (base, spread) in spreads.items():
        noise = np.random.default_rng([zlib.crc32(name.encode()), seed]).standard_normal(out[name].shape)
        drawn = base * np.exp(spread * noise) if base else spread * noise
        out[name] = jnp.asarray(drawn.astype(out[name].dtype))
    for name, factor in factors.items():
        out[name] = (out[name] * factor).astype(out[name].dtype)
    return out
```

```python
import numpy as np

import concourse.bass as bass
from concourse import mybir
from concourse.alu_op_type import AluOpType as ALU

F32 = mybir.dt.float32
F32R = mybir.dt.float32r
I32 = mybir.dt.int32
ACT = mybir.ActivationFunctionType
AX = mybir.AxisListType

P = 128
LEAD_K = 5
LEAD_Q = 2
LEAD_X = 3
LEAD_V = 2
LAG_PT = 1
LAG_O = 2
UNROLL = 8
FIRST = 11


def attention(nc, x, f, stage, embed, out):
    B, S, D = x.shape
    C = S // P
    N = B * C
    STAGES = embed.shape[0]
    assert S == D == C * P and C == 4 and N % UNROLL == 0
    ROUNDS = (N - LEAD_K - FIRST + 1) // UNROLL
    LAST = N - 1 + LAG_O

    x_rows = x.rearrange("b (p i) d -> b p i d", i=C)
    out_rows = out.rearrange("b (p i) d -> b p i d", i=C)
    f_rows = f.rearrange("b (p j) d -> b p j d", j=C)

    def sb(name, shape, dt=F32):
        return nc.alloc_sbuf_tensor(name, shape, dt)

    x_sb = sb("x_sb", [P, 2 * C, D])
    k_sb = sb("k_sb", [P, 2, C, D])
    q_sb = sb("q_sb", [P, 2, D])
    qT_hi = sb("qT_hi", [P, 4, C, P], F32R)
    qT_lo = sb("qT_lo", [P, 4, C, P], F32R)
    kT_hi = sb("kT_hi", [P, 2, C, S], F32R)
    kT_lo = sb("kT_lo", [P, 2, C, S], F32R)
    v_hi = sb("v_hi", [P, 2, C, D], F32R)
    v_lo = sb("v_lo", [P, 2, C, D], F32R)
    p_sb = sb("p_sb", [P, 2, S])
    pT_hi = sb("pT_hi", [P, 2, C, P], F32R)
    pT_lo = sb("pT_lo", [P, 2, C, P], F32R)
    negmax = sb("negmax", [P, 4])
    rowsum = sb("rowsum", [P, 4])
    rowinv = sb("rowinv", [P, 4])
    o_sb = sb("o_sb", [P, 4, D])
    bias = sb("bias", [P, C, B])
    ident = sb("ident", [P, P])
    embed_sb = sb("embed_sb", [STAGES, S])
    stage_i = sb("stage_i", [STAGES, B], I32)
    stage_f = sb("stage_f", [STAGES, B])
    wrap = sb("wrap", [STAGES, B])
    onehot = sb("onehot", [STAGES, B])
    own_i = sb("own_i", [STAGES, 1], I32)
    own_f = sb("own_f", [STAGES, 1])

    ps_s = [nc.alloc_psum_tensor(f"ps_s{n}", [P, S], F32) for n in range(2)]
    ps_o = [nc.alloc_psum_tensor(f"ps_o{n}", [P, D], F32) for n in range(2)]
    ps_pT = [nc.alloc_psum_tensor(f"ps_pT{n}", [P, C, P], F32) for n in range(2)]
    ps_q = nc.alloc_psum_tensor("ps_q", [P, C, P], F32)
    ps_k = nc.alloc_psum_tensor("ps_k", [P, S], F32)
    ps_bias = ps_o[0]

    sem = nc.alloc_semaphore
    table_loaded = sem("table_loaded")
    ident_ready = sem("ident_ready")
    own_ready = sem("own_ready")
    setup_step = sem("setup_step")
    onehot_ready = sem("onehot_ready")
    bias_in_psum = sem("bias_in_psum")
    bias_ready = sem("bias_ready")
    x_loaded = [sem(f"x_loaded{n}") for n in range(4)]
    k_loaded = [sem(f"k_loaded{n}") for n in range(2)]
    q_ready = sem("q_ready")
    qT_done = sem("qT_done")
    qhi_done = sem("qhi_done")
    qlo_done = sem("qlo_done")
    kT_done = sem("kT_done")
    khi_done = sem("khi_done")
    klo_done = sem("klo_done")
    vhi_done = sem("vhi_done")
    vlo_done = sem("vlo_done")
    scores_done = sem("scores_done")
    max_done = sem("max_done")
    exp_done = sem("exp_done")
    pT_done = sem("pT_done")
    phi_done = sem("phi_done")
    plo_done = sem("plo_done")
    inv_done = sem("inv_done")
    values_done = sem("values_done")
    out_done = sem("out_done")
    stored = [sem(f"stored{n}") for n in range(2)]

    def wait(eng, s, m, per_round, c):
        if isinstance(m, int):
            if per_round * m + c > 0:
                eng.wait_ge(s, per_round * m + c)
        else:
            assert c > 0, "a wait in a loop starts at zero or below"
            eng.wait_ge(s, m * per_round + c)

    def exists(m, c):
        return 0 <= UNROLL * m + c < N if isinstance(m, int) else True

    def run_steps(eng, step):
        for c in range(FIRST):
            step(0, c)
        with eng.Fori(0, ROUNDS) as m:
            for c in range(FIRST, FIRST + UNROLL):
                step(m, c)
        for c in range(FIRST, LAST + 1 - UNROLL * ROUNDS):
            step(ROUNDS, c)

    with nc.Block() as block:

        @block.sync
        def _(sp):
            def load_x(b, half):
                slot = 2 * (b[1] % 2) + half
                sp.dma_start(x_sb[:, 2 * slot:2 * slot + 2, :],
                             x_rows[b[0] + b[1], :, 2 * half:2 * half + 2, :]).then_inc(x_loaded[slot], 16)

            def load_k(b):
                sp.dma_start(k_sb[:, b[1] % 2, :, :], f_rows[b[0] + b[1], :, :, :]).then_inc(k_loaded[b[1] % 2], 16)

            def round_(m):
                for j in range(4):
                    if j % 2 == 0:
                        b = (2 * m, j // 2 + 2)
                        wait(sp, kT_done, m, 8, 4 * (j // 2 + 1))
                        wait(sp, vhi_done, m, 8, 4 * (j // 2 + 1))
                        wait(sp, vlo_done, m, 8, 4 * (j // 2 + 1))
                        load_k(b)
                    store(m, j)
                    load_x((2 * m, 2 + j // 2), j % 2)

            def store(m, j):
                wait(sp, out_done, m, 8, 2 * j + 2)
                half = j % 2
                sp.dma_start(out_rows[2 * m + j // 2, :, 2 * half:2 * half + 2, :],
                             o_sb[:, 2 * half:2 * half + 2, :]).then_inc(stored[half], 16)

            load_k((0, 0))
            load_x((0, 0), 0)
            sp.dma_start(stage_i[:, :], stage.rearrange("(a b) -> a b", a=1).broadcast_to([STAGES, B])
                         ).then_inc(table_loaded, 16)
            sp.dma_start(embed_sb[:, :], embed).then_inc(table_loaded, 16)
            load_x((0, 0), 1)
            load_k((0, 1))
            load_x((0, 1), 0)
            load_x((0, 1), 1)
            with sp.Fori(0, N // UNROLL - 1) as m:
                round_(m)
            for j in range(4):
                store(N // UNROLL - 1, j)
            for half in range(2):
                sp.wait_ge(stored[half], 16 * (N // 4))

        @block.gpsimd
        def _(pool):
            pool.memset(ident[:, :], 0.0).then_inc(ident_ready, 1)
            pool.iota(own_i[:, :], pattern=[[0, 1]], base=0, channel_multiplier=1).then_inc(own_ready, 1)
            pool.wait_ge(ident_ready, 1)
            pool.affine_select(out=ident[:, :], in_=ident[:, :], compare_op=ALU.not_equal, fill=1.0,
                               base=0, pattern=[[-1, P]], channel_multiplier=1).then_inc(ident_ready, 1)

            def split_values(m, c):
                if not exists(m, c):
                    return
                half, j = c // C % 2, c % C
                wait(pool, vhi_done, m, 8, c + 1)
                pool.tensor_tensor(v_lo[:, half, j, :], k_sb[:, half, j, :], v_hi[:, half, j, :].bitcast(F32),
                                   ALU.subtract).then_inc(vlo_done, 1)

            for c in range(LEAD_V):
                split_values(0, c)
            run_steps(pool, lambda m, c: split_values(m, c + LEAD_V))

        @block.scalar
        def _(act):
            def add_bias(m, c):
                if not exists(m, c):
                    return
                b, i = c // C, c % C
                if i % 2 == 0:
                    slot = c // 2 % 4
                    wait(act, x_loaded[slot], m, 16, 16 * (c // 8 + 1))
                wait(act, qT_done, m, 8, c - 1)
                act.activation(q_sb[:, c % 2, :], x_sb[:, c % 8, :], ACT.Identity,
                               bias=bias[:, i, bass.ds(2 * m + b, 1)]).then_inc(q_ready, 1)

            def high_queries(m, c):
                if not exists(m, c):
                    return
                wait(act, qT_done, m, 8, c + 1)
                wait(act, scores_done, m, 8, c - 3)
                act.activation(qT_hi[:, c % 4, :, :], ps_q[:, :, :], ACT.Copy).then_inc(qhi_done, 1)

            def high_keys(m, c):
                if not exists(m, c):
                    return
                b, j = c // C, c % C
                wait(act, kT_done, m, 8, c + 1)
                if j == 0:
                    wait(act, scores_done, m, 8, 4 * (b - 1))
                act.activation(kT_hi[:, b % 2, j, :], ps_k[:, :], ACT.Copy).then_inc(khi_done, 1)

            def high_probabilities(m, c):
                if not exists(m, c):
                    return
                wait(act, pT_done, m, 8, c + 1)
                wait(act, values_done, m, 8, c - 1)
                act.activation(pT_hi[:, c % 2, :, :], ps_pT[c % 2][:, :, :], ACT.Copy).then_inc(phi_done, 1)

            def exponentials(m, c):
                if not exists(m, c):
                    return
                wait(act, max_done, m, 8, c + 1)
                wait(act, pT_done, m, 8, c - 1)
                wait(act, inv_done, m, 8, c - 3)
                act.activation(p_sb[:, c % 2, :], ps_s[c % 2][:, :], ACT.Exp, bias=negmax[:, c % 4:c % 4 + 1],
                               accum_out=rowsum[:, c % 4:c % 4 + 1]).then_inc(exp_done, 1)

            def step(m, c):
                high_probabilities(m, c - LAG_PT)
                high_keys(m, c + LEAD_K)
                high_queries(m, c + LEAD_Q)
                exponentials(m, c)
                add_bias(m, c + LEAD_X)

            act.wait_ge(bias_ready, 1)
            for c in range(LEAD_Q):
                add_bias(0, c)
            for c in range(C):
                high_keys(0, c)
            for c in range(LEAD_Q):
                high_queries(0, c)
            for c in range(LEAD_Q, LEAD_X):
                add_bias(0, c)
            high_keys(0, C)
            run_steps(act, step)

        @block.vector
        def _(dve):
            dve.wait_ge(table_loaded, 32)
            dve.tensor_copy(stage_f[:, :], stage_i[:, :]).then_inc(setup_step, 1)
            dve.wait_ge(own_ready, 1)
            dve.tensor_copy(own_f[:, :], own_i[:, :]).then_inc(setup_step, 1)
            dve.wait_ge(setup_step, 2)
            dve.tensor_scalar(wrap[:, :], stage_f[:, :], 0.0, float(STAGES), ALU.is_lt, ALU.mult
                              ).then_inc(setup_step, 1)
            dve.wait_ge(setup_step, 3)
            dve.tensor_tensor(stage_f[:, :], stage_f[:, :], wrap[:, :], ALU.add).then_inc(setup_step, 1)
            dve.wait_ge(setup_step, 4)
            dve.tensor_scalar(wrap[:, :], stage_f[:, :], 0.0, float(STAGES - 1), ALU.max, ALU.min
                              ).then_inc(setup_step, 1)
            dve.wait_ge(setup_step, 5)
            dve.tensor_scalar(onehot[:, :], wrap[:, :], own_f[:, 0:1], None, ALU.is_equal
                              ).then_inc(onehot_ready, 1)
            dve.wait_ge(bias_in_psum, 1)
            dve.tensor_copy(bias[:, :, :], ps_bias[:, 0:C * B].rearrange("p (i b) -> p i b", i=C)
                            ).then_inc(bias_ready, 1)

            def low(m, c, dst, src, hi, done, hi_done):
                wait(dve, hi_done, m, 8, c + 1)
                dve.tensor_tensor(dst, src, hi.bitcast(F32), ALU.subtract).then_inc(done, 1)

            def low_queries(m, c):
                if exists(m, c):
                    low(m, c, qT_lo[:, c % 4, :, :], ps_q[:, :, :], qT_hi[:, c % 4, :, :], qlo_done, qhi_done)

            def low_keys(m, c):
                if exists(m, c):
                    b, j = c // C % 2, c % C
                    low(m, c, kT_lo[:, b, j, :], ps_k[:, :], kT_hi[:, b, j, :], klo_done, khi_done)

            def low_probabilities(m, c):
                if exists(m, c):
                    low(m, c, pT_lo[:, c % 2, :, :], ps_pT[c % 2][:, :, :], pT_hi[:, c % 2, :, :], plo_done, phi_done)

            def high_values(m, c):
                if not exists(m, c):
                    return
                b, j = c // C, c % C
                if j == 0:
                    wait(dve, k_loaded[b % 2], m, 16, 16 * (b // 2 + 1))
                    wait(dve, values_done, m, 8, 4 * (b - 1))
                dve.tensor_copy(v_hi[:, b % 2, j, :], k_sb[:, b % 2, j, :]).then_inc(vhi_done, 1)

            def maximum(m, c):
                if not exists(m, c):
                    return
                wait(dve, scores_done, m, 8, c + 1)
                wait(dve, exp_done, m, 8, c - 3)
                dve.reduce_max(negmax[:, c % 4:c % 4 + 1], ps_s[c % 2][:, :], axis=AX.X, negate=True
                               ).then_inc(max_done, 1)

            def inverse(m, c):
                if not exists(m, c):
                    return
                wait(dve, exp_done, m, 8, c + 1)
                dve.reciprocal(rowinv[:, c % 4:c % 4 + 1], rowsum[:, c % 4:c % 4 + 1]).then_inc(inv_done, 1)

            def result(m, c):
                if not exists(m, c):
                    return
                wait(dve, values_done, m, 8, c + 1)
                wait(dve, inv_done, m, 8, c + 1)
                if c % 2 == 0:
                    wait(dve, stored[c // 2 % 2], m, 32, 16 * (c // 4))
                dve.scalar_tensor_tensor(o_sb[:, c % 4, :], ps_o[c % 2][:, :], rowinv[:, c % 4:c % 4 + 1],
                                         x_sb[:, c % 8, :], ALU.mult, ALU.add).then_inc(out_done, 1)

            def step(m, c):
                maximum(m, c)
                low_probabilities(m, c - LAG_PT)
                low_keys(m, c + LEAD_K)
                low_queries(m, c + LEAD_Q)
                inverse(m, c - LAG_PT)
                high_values(m, c + LEAD_V)
                result(m, c - LAG_O)

            for c in range(C):
                low_keys(0, c)
            for c in range(LEAD_Q):
                low_queries(0, c)
            for c in range(LEAD_V):
                high_values(0, c)
            low_keys(0, C)
            run_steps(dve, step)

        @block.tensor
        def _(pe):
            def split_product(bank, lhs_hi, lhs_lo, rhs_hi, rhs_lo):
                terms = [t for n in range(C) for t in
                         ((lhs_lo[n], rhs_hi[n]), (lhs_hi[n], rhs_lo[n]), (lhs_hi[n], rhs_hi[n]))]
                for n, (lhs, rhs) in enumerate(terms):
                    last = pe.matmul(bank, lhs, rhs, start=(n == 0), stop=(n == len(terms) - 1))
                return last

            def scores(m, c):
                if not exists(m, c):
                    return
                b = c // C
                wait(pe, qlo_done, m, 8, c + 1)
                if c % C == 0:
                    wait(pe, klo_done, m, 8, 4 * (b + 1))
                wait(pe, exp_done, m, 8, c - 1)
                split_product(ps_s[c % 2][:, :],
                              [qT_hi[:, c % 4, n, :] for n in range(C)], [qT_lo[:, c % 4, n, :] for n in range(C)],
                              [kT_hi[:, b % 2, n, :] for n in range(C)], [kT_lo[:, b % 2, n, :] for n in range(C)]
                              ).then_inc(scores_done, 1)

            def transpose_probabilities(m, c):
                if not exists(m, c):
                    return
                wait(pe, exp_done, m, 8, c + 1)
                wait(pe, plo_done, m, 8, c - 1)
                for n in range(C):
                    last = pe.transpose(ps_pT[c % 2][:, n, :], p_sb[:, c % 2, n * P:(n + 1) * P], ident[:, :])
                last.then_inc(pT_done, 1)

            def transpose_keys(m, c):
                if not exists(m, c):
                    return
                b, j = c // C, c % C
                if j == 0:
                    wait(pe, k_loaded[b % 2], m, 16, 16 * (b // 2 + 1))
                wait(pe, klo_done, m, 8, c)
                for n in range(C):
                    last = pe.transpose(ps_k[:, n * P:(n + 1) * P], k_sb[:, b % 2, n, j * P:(j + 1) * P], ident[:, :])
                last.then_inc(kT_done, 1)

            def transpose_queries(m, c):
                if not exists(m, c):
                    return
                wait(pe, q_ready, m, 8, c + 1)
                wait(pe, qlo_done, m, 8, c)
                for n in range(C):
                    last = pe.transpose(ps_q[:, n, :], q_sb[:, c % 2, n * P:(n + 1) * P], ident[:, :])
                last.then_inc(qT_done, 1)

            def values(m, c):
                if not exists(m, c):
                    return
                b = c // C
                wait(pe, plo_done, m, 8, c + 1)
                if c % C == 0:
                    wait(pe, vlo_done, m, 8, 4 * (b + 1))
                wait(pe, out_done, m, 8, c - 1)
                split_product(ps_o[c % 2][:, :],
                              [pT_hi[:, c % 2, n, :] for n in range(C)], [pT_lo[:, c % 2, n, :] for n in range(C)],
                              [v_hi[:, b % 2, n, :] for n in range(C)], [v_lo[:, b % 2, n, :] for n in range(C)]
                              ).then_inc(values_done, 1)

            def step(m, c):
                scores(m, c)
                transpose_probabilities(m, c - LAG_PT)
                transpose_keys(m, c + LEAD_K)
                transpose_queries(m, c + LEAD_Q)
                values(m, c - LAG_O)

            pe.wait_ge(onehot_ready, 1)
            rows = embed_sb[:, :].rearrange("n (p i) -> n i p", i=C)
            for i in range(C):
                last = pe.matmul(ps_bias[:, i * B:(i + 1) * B], rows[:, i, :], onehot[:, :], start=True, stop=True)
            last.then_inc(bias_in_psum, 1)
            pe.wait_ge(ident_ready, 2)
            for c in range(C):
                transpose_keys(0, c)
            for c in range(LEAD_Q):
                transpose_queries(0, c)
            transpose_keys(0, C)
            run_steps(pe, step)


def kernel(**inputs):
    import concourse.bacc as bacc
    from concourse.bass_utils import run_bass_kernel_spmd

    nc = bacc.Bacc("TRN2", target_bir_lowering=False, num_devices=1)
    names = ["x", "fside_BxSxS_0", "itok_B_0_5", "L0_cond_braak_embed"]
    arrays = {f"in_{n}": np.ascontiguousarray(inputs[n]) for n in names}
    args = [nc.dram_tensor(n, a.shape, mybir.dt.from_np(a.dtype), kind="ExternalInput").ap()
            for n, a in arrays.items()]
    out = nc.dram_tensor("out", arrays["in_x"].shape, F32, kind="ExternalOutput").ap()
    attention(nc, *args, out)
    result = run_bass_kernel_spmd(nc, [arrays], core_ids=[0])
    return result.results[0]["out"]
```

```python
import numpy as np

import concourse.bass as bass
from concourse import mybir
from concourse.alu_op_type import AluOpType as ALU

F32 = mybir.dt.float32
F32R = mybir.dt.float32r
I32 = mybir.dt.int32
ACT = mybir.ActivationFunctionType
AX = mybir.AxisListType

P = 128
Q = 32
LEAD_K = 5
LEAD_Q = 2
LEAD_X = 3
LEAD_V = 2
LAG_PT = 1
LAG_O = 2
UNROLL = 8
FIRST = 11


def attention(nc, x, f, stage, embed, out):
    B, S, D = x.shape
    C = S // P
    R = S // Q
    N = B * C
    STAGES = embed.shape[0]
    assert S == D == C * P and C == 4 and N % UNROLL == 0
    ROUNDS = (N - LEAD_K - FIRST + 1) // UNROLL
    LAST = N - 1 + LAG_O

    x_rows = x.rearrange("b (i p) d -> b p i d", p=P)
    out_rows = out.rearrange("b (i p) d -> b p i d", p=P)
    f_rows = f.rearrange("b (j p) d -> b p j d", p=P)
    x_blocks = x.rearrange("b (r t) (a n) -> b a t r n", t=Q, a=C)
    f_blocks = f.rearrange("b (r t) (a n) -> b a t r n", t=Q, a=C)

    def sb(name, shape, dt=F32):
        return nc.alloc_sbuf_tensor(name, shape, dt)

    x_sb = sb("x_sb", [P, 2 * C, D])
    k_sb = sb("k_sb", [P, 2, C, D])
    xb_sb = sb("xb_sb", [P, 2, R, P])
    kb_sb = sb("kb_sb", [P, 2, R, P])
    qT_hi = sb("qT_hi", [P, 4, C, P], F32R)
    qT_lo = sb("qT_lo", [P, 4, C, P], F32R)
    kT_hi = sb("kT_hi", [P, 2, C, S], F32R)
    kT_lo = sb("kT_lo", [P, 2, C, S], F32R)
    v_hi = sb("v_hi", [P, 2, C, D], F32R)
    v_lo = sb("v_lo", [P, 2, C, D], F32R)
    p_sb = sb("p_sb", [P, 2, S])
    pT_hi = sb("pT_hi", [P, 2, C, P], F32R)
    pT_lo = sb("pT_lo", [P, 2, C, P], F32R)
    negmax = sb("negmax", [P, 4])
    rowsum = sb("rowsum", [P, 4])
    rowinv = sb("rowinv", [P, 4])
    o_sb = sb("o_sb", [P, 4, D])
    bias = sb("bias", [P, R, B])
    ident = sb("ident", [P, P])
    embed_sb = sb("embed_sb", [STAGES, R, C, Q])
    stage_i = sb("stage_i", [STAGES, B], I32)
    stage_f = sb("stage_f", [STAGES, B])
    wrap = sb("wrap", [STAGES, B])
    onehot = sb("onehot", [STAGES, B])
    own_i = sb("own_i", [STAGES, 1], I32)
    own_f = sb("own_f", [STAGES, 1])

    ps_s = [nc.alloc_psum_tensor(f"ps_s{n}", [P, S], F32) for n in range(2)]
    ps_o = [nc.alloc_psum_tensor(f"ps_o{n}", [P, D], F32) for n in range(2)]
    ps_pT = [nc.alloc_psum_tensor(f"ps_pT{n}", [P, C, P], F32) for n in range(2)]
    ps_q = nc.alloc_psum_tensor("ps_q", [P, C, P], F32)
    ps_k = nc.alloc_psum_tensor("ps_k", [P, S], F32)
    ps_bias = ps_o[0]

    sem = nc.alloc_semaphore
    table_loaded = sem("table_loaded")
    ident_ready = sem("ident_ready")
    own_ready = sem("own_ready")
    setup_step = sem("setup_step")
    onehot_ready = sem("onehot_ready")
    bias_in_psum = sem("bias_in_psum")
    bias_ready = sem("bias_ready")
    x_loaded = [sem(f"x_loaded{n}") for n in range(4)]
    k_loaded = [sem(f"k_loaded{n}") for n in range(2)]
    xb_loaded = [sem(f"xb_loaded{n}") for n in range(4)]
    kb_loaded = [sem(f"kb_loaded{n}") for n in range(2)]
    q_ready = sem("q_ready")
    qT_done = sem("qT_done")
    qhi_done = sem("qhi_done")
    qlo_done = sem("qlo_done")
    kT_done = sem("kT_done")
    khi_done = sem("khi_done")
    klo_done = sem("klo_done")
    vhi_done = sem("vhi_done")
    vlo_done = sem("vlo_done")
    scores_done = sem("scores_done")
    max_done = sem("max_done")
    exp_done = sem("exp_done")
    pT_done = sem("pT_done")
    phi_done = sem("phi_done")
    plo_done = sem("plo_done")
    inv_done = sem("inv_done")
    values_done = sem("values_done")
    out_done = sem("out_done")
    stored = [sem(f"stored{n}") for n in range(2)]

    def wait(eng, s, m, per_round, c):
        if isinstance(m, int):
            if per_round * m + c > 0:
                eng.wait_ge(s, per_round * m + c)
        else:
            assert c > 0, "a wait in a loop starts at zero or below"
            eng.wait_ge(s, m * per_round + c)

    def exists(m, c):
        return 0 <= UNROLL * m + c < N if isinstance(m, int) else True

    def run_steps(eng, step):
        for c in range(FIRST):
            step(0, c)
        with eng.Fori(0, ROUNDS) as m:
            for c in range(FIRST, FIRST + UNROLL):
                step(m, c)
        for c in range(FIRST, LAST + 1 - UNROLL * ROUNDS):
            step(ROUNDS, c)

    with nc.Block() as block:

        @block.sync
        def _(sp):
            def load_x(m, j):
                b, half, slot = 2 * m + j // 2, j % 2, j % 4
                sp.dma_start(x_sb[:, 2 * slot:2 * slot + 2, :], x_rows[b, :, 2 * half:2 * half + 2, :]
                             ).then_inc(x_loaded[slot], 16)

            def load_x_blocks(m, j):
                b, half, slot = 2 * m + j // 2, j % 2, j % 4
                rows = slice(R // 2 * half, R // 2 * (half + 1))
                for a in range(C):
                    sp.dma_start(xb_sb[Q * a:Q * a + Q, slot // 2, rows, :], x_blocks[b, a, :, rows, :]
                                 ).then_inc(xb_loaded[slot], 16)

            def load_keys(m, b):
                sp.dma_start(k_sb[:, b % 2, :, :], f_rows[2 * m + b, :, :, :]).then_inc(k_loaded[b % 2], 16)

            def load_key_blocks(m, b):
                for a in range(C):
                    sp.dma_start(kb_sb[Q * a:Q * a + Q, b % 2, :, :], f_blocks[2 * m + b, a, :, :, :]
                                 ).then_inc(kb_loaded[b % 2], 16)

            def store(m, j):
                wait(sp, out_done, m, 8, 2 * j + 2)
                half = j % 2
                sp.dma_start(out_rows[2 * m + j // 2, :, 2 * half:2 * half + 2, :],
                             o_sb[:, 2 * half:2 * half + 2, :]).then_inc(stored[half], 16)

            def round_(m, last=False):
                for j in range(4):
                    if not last:
                        wait(sp, qT_done, m, 8, 2 * j + 2)
                        load_x_blocks(m, j + 4)
                        if j % 2 == 0:
                            b = j // 2
                            wait(sp, kT_done, m, 8, 4 * b + 4)
                            load_key_blocks(m, b + 2)
                            wait(sp, vlo_done, m, 8, 4 * b + 4)
                            load_keys(m, b + 2)
                    store(m, j)
                    if not last:
                        load_x(m, j + 4)

            load_key_blocks(0, 0)
            for a in range(C):
                sp.dma_start(embed_sb[:, :, a, :], embed.rearrange("n (r t) -> n r t", t=Q)
                             ).then_inc(table_loaded, 16)
            sp.dma_start(stage_i[:, :], stage.rearrange("(a b) -> a b", a=1).broadcast_to([STAGES, B])
                         ).then_inc(table_loaded, 16)
            load_x_blocks(0, 0)
            load_keys(0, 0)
            load_key_blocks(0, 1)
            load_x_blocks(0, 1)
            load_x(0, 0)
            load_x(0, 1)
            load_x_blocks(0, 2)
            load_keys(0, 1)
            load_x_blocks(0, 3)
            load_x(0, 2)
            load_x(0, 3)
            with sp.Fori(0, N // UNROLL - 1) as m:
                round_(m)
            round_(N // UNROLL - 1, last=True)
            for half in range(2):
                sp.wait_ge(stored[half], 16 * (N // 4))

        @block.gpsimd
        def _(pool):
            pool.memset(ident[:, :], 0.0).then_inc(ident_ready, 1)
            pool.iota(own_i[:, :], pattern=[[0, 1]], base=0, channel_multiplier=1).then_inc(own_ready, 1)
            pool.wait_ge(ident_ready, 1)
            pool.affine_select(out=ident[:, :], in_=ident[:, :], compare_op=ALU.not_equal, fill=1.0,
                               base=0, pattern=[[-1, P]], channel_multiplier=1).then_inc(ident_ready, 1)

            def split_values(m, c):
                if not exists(m, c):
                    return
                half, j = c // C % 2, c % C
                wait(pool, vhi_done, m, 8, c + 1)
                pool.tensor_tensor(v_lo[:, half, j, :], k_sb[:, half, j, :], v_hi[:, half, j, :].bitcast(F32),
                                   ALU.subtract).then_inc(vlo_done, 1)

            def add_bias(m, c):
                if not exists(m, c):
                    return
                if c % 2 == 0:
                    wait(pool, xb_loaded[c // 2 % 4], m, 64, 64 * (c // 8 + 1))
                half, rows = c // C % 2, slice(c % C * C, c % C * C + C)
                tile = xb_sb[:, half, rows, :]
                pool.tensor_tensor(tile, tile, bias[:, rows, bass.ds(2 * m + c // C, 1)].to_broadcast([P, C, P]),
                                   ALU.add).then_inc(q_ready, 1)

            def step(m, c):
                add_bias(m, c + LEAD_X)
                split_values(m, c + LEAD_V)

            pool.wait_ge(bias_ready, 1)
            for c in range(LEAD_X):
                add_bias(0, c)
            for c in range(LEAD_V):
                split_values(0, c)
            run_steps(pool, step)

        @block.scalar
        def _(act):
            def high_queries(m, c):
                if not exists(m, c):
                    return
                wait(act, qT_done, m, 8, c + 1)
                wait(act, scores_done, m, 8, c - 3)
                act.activation(qT_hi[:, c % 4, :, :], ps_q[:, :, :], ACT.Copy).then_inc(qhi_done, 1)

            def high_keys(m, c):
                if not exists(m, c):
                    return
                b, j = c // C, c % C
                wait(act, kT_done, m, 8, c + 1)
                if j == 0:
                    wait(act, scores_done, m, 8, 4 * (b - 1))
                act.activation(kT_hi[:, b % 2, j, :], ps_k[:, :], ACT.Copy).then_inc(khi_done, 1)

            def high_values(m, c):
                if not exists(m, c):
                    return
                b, j = c // C, c % C
                if j == 0:
                    wait(act, k_loaded[b % 2], m, 16, 16 * (b // 2 + 1))
                    wait(act, values_done, m, 8, 4 * (b - 1))
                act.activation(v_hi[:, b % 2, j, :], k_sb[:, b % 2, j, :], ACT.Copy).then_inc(vhi_done, 1)

            def high_probabilities(m, c):
                if not exists(m, c):
                    return
                wait(act, pT_done, m, 8, c + 1)
                wait(act, values_done, m, 8, c - 1)
                act.activation(pT_hi[:, c % 2, :, :], ps_pT[c % 2][:, :, :], ACT.Copy).then_inc(phi_done, 1)

            def exponentials(m, c):
                if not exists(m, c):
                    return
                wait(act, max_done, m, 8, c + 1)
                wait(act, pT_done, m, 8, c - 1)
                wait(act, inv_done, m, 8, c - 3)
                act.activation(p_sb[:, c % 2, :], ps_s[c % 2][:, :], ACT.Exp, bias=negmax[:, c % 4:c % 4 + 1],
                               accum_out=rowsum[:, c % 4:c % 4 + 1]).then_inc(exp_done, 1)

            def step(m, c):
                high_keys(m, c + LEAD_K)
                high_queries(m, c + LEAD_Q)
                high_probabilities(m, c - LAG_PT)
                exponentials(m, c)
                high_values(m, c + LEAD_V)

            for c in range(LEAD_Q):
                high_keys(0, c)
                high_queries(0, c)
            for c in range(LEAD_Q, LEAD_K):
                high_keys(0, c)
            for c in range(LEAD_V):
                high_values(0, c)
            run_steps(act, step)

        @block.vector
        def _(dve):
            dve.wait_ge(table_loaded, 16 * (C + 1))
            dve.tensor_copy(stage_f[:, :], stage_i[:, :]).then_inc(setup_step, 1)
            dve.wait_ge(own_ready, 1)
            dve.tensor_copy(own_f[:, :], own_i[:, :]).then_inc(setup_step, 1)
            dve.wait_ge(setup_step, 2)
            dve.tensor_scalar(wrap[:, :], stage_f[:, :], 0.0, float(STAGES), ALU.is_lt, ALU.mult
                              ).then_inc(setup_step, 1)
            dve.wait_ge(setup_step, 3)
            dve.tensor_tensor(stage_f[:, :], stage_f[:, :], wrap[:, :], ALU.add).then_inc(setup_step, 1)
            dve.wait_ge(setup_step, 4)
            dve.tensor_scalar(wrap[:, :], stage_f[:, :], 0.0, float(STAGES - 1), ALU.max, ALU.min
                              ).then_inc(setup_step, 1)
            dve.wait_ge(setup_step, 5)
            dve.tensor_scalar(onehot[:, :], wrap[:, :], own_f[:, 0:1], None, ALU.is_equal
                              ).then_inc(onehot_ready, 1)
            dve.wait_ge(bias_in_psum, 1)
            dve.tensor_copy(bias[:, :, :], ps_bias[:, :].rearrange("p (r b) -> p r b", r=R)
                            ).then_inc(bias_ready, 1)

            def transpose_keys(m, c):
                if not exists(m, c):
                    return
                b, j = c // C, c % C
                if j == 0:
                    wait(dve, kb_loaded[b % 2], m, 64, 64 * (b // 2 + 1))
                wait(dve, klo_done, m, 8, c)
                dve.transpose(ps_k[:, :], kb_sb[:, b % 2, :, Q * j:Q * j + Q]).then_inc(kT_done, 1)

            def transpose_queries(m, c):
                if not exists(m, c):
                    return
                wait(dve, q_ready, m, 8, c + 1)
                wait(dve, qlo_done, m, 8, c)
                rows = slice(c % C * C, c % C * C + C)
                dve.transpose(ps_q[:, :, :].rearrange("p c (r s) -> p r c s", s=Q),
                              xb_sb[:, c // C % 2, rows, :].rearrange("p r (c u) -> p r c u", u=Q)
                              ).then_inc(qT_done, 1)

            def low(m, c, dst, src, hi, done, hi_done):
                wait(dve, hi_done, m, 8, c + 1)
                dve.tensor_tensor(dst, src, hi.bitcast(F32), ALU.subtract).then_inc(done, 1)

            def low_queries(m, c):
                if exists(m, c):
                    low(m, c, qT_lo[:, c % 4, :, :], ps_q[:, :, :], qT_hi[:, c % 4, :, :], qlo_done, qhi_done)

            def low_keys(m, c):
                if exists(m, c):
                    b, j = c // C % 2, c % C
                    low(m, c, kT_lo[:, b, j, :], ps_k[:, :], kT_hi[:, b, j, :], klo_done, khi_done)

            def low_probabilities(m, c):
                if exists(m, c):
                    low(m, c, pT_lo[:, c % 2, :, :], ps_pT[c % 2][:, :, :], pT_hi[:, c % 2, :, :], plo_done, phi_done)

            def maximum(m, c):
                if not exists(m, c):
                    return
                wait(dve, scores_done, m, 8, c + 1)
                wait(dve, exp_done, m, 8, c - 3)
                dve.reduce_max(negmax[:, c % 4:c % 4 + 1], ps_s[c % 2][:, :], axis=AX.X, negate=True
                               ).then_inc(max_done, 1)

            def inverse(m, c):
                if not exists(m, c):
                    return
                wait(dve, exp_done, m, 8, c + 1)
                dve.reciprocal(rowinv[:, c % 4:c % 4 + 1], rowsum[:, c % 4:c % 4 + 1]).then_inc(inv_done, 1)

            def result(m, c):
                if not exists(m, c):
                    return
                wait(dve, values_done, m, 8, c + 1)
                wait(dve, inv_done, m, 8, c + 1)
                if c % 2 == 0:
                    wait(dve, stored[c // 2 % 2], m, 32, 16 * (c // 4))
                dve.scalar_tensor_tensor(o_sb[:, c % 4, :], ps_o[c % 2][:, :], rowinv[:, c % 4:c % 4 + 1],
                                         x_sb[:, c % 8, :], ALU.mult, ALU.add).then_inc(out_done, 1)

            def step(m, c):
                transpose_keys(m, c + LEAD_K)
                transpose_queries(m, c + LEAD_Q)
                maximum(m, c)
                low_keys(m, c + LEAD_K)
                low_queries(m, c + LEAD_Q)
                low_probabilities(m, c - LAG_PT)
                inverse(m, c - LAG_PT)
                result(m, c - LAG_O)

            for c in range(LEAD_Q):
                transpose_keys(0, c)
                transpose_queries(0, c)
                low_keys(0, c)
                low_queries(0, c)
            for c in range(LEAD_Q, LEAD_K):
                transpose_keys(0, c)
                low_keys(0, c)
            run_steps(dve, step)

        @block.tensor
        def _(pe):
            def split_product(bank, lhs_hi, lhs_lo, rhs_hi, rhs_lo):
                terms = [t for n in range(C) for t in
                         ((lhs_lo[n], rhs_hi[n]), (lhs_hi[n], rhs_lo[n]), (lhs_hi[n], rhs_hi[n]))]
                for n, (lhs, rhs) in enumerate(terms):
                    last = pe.matmul(bank, lhs, rhs, start=(n == 0), stop=(n == len(terms) - 1))
                return last

            def scores(m, c):
                if not exists(m, c):
                    return
                b = c // C
                wait(pe, qlo_done, m, 8, c + 1)
                if c % C == 0:
                    wait(pe, klo_done, m, 8, 4 * (b + 1))
                wait(pe, exp_done, m, 8, c - 1)
                split_product(ps_s[c % 2][:, :],
                              [qT_hi[:, c % 4, n, :] for n in range(C)], [qT_lo[:, c % 4, n, :] for n in range(C)],
                              [kT_hi[:, b % 2, n, :] for n in range(C)], [kT_lo[:, b % 2, n, :] for n in range(C)]
                              ).then_inc(scores_done, 1)

            def transpose_probabilities(m, c):
                if not exists(m, c):
                    return
                wait(pe, exp_done, m, 8, c + 1)
                wait(pe, plo_done, m, 8, c - 1)
                for n in range(C):
                    last = pe.transpose(ps_pT[c % 2][:, n, :], p_sb[:, c % 2, n * P:(n + 1) * P], ident[:, :])
                last.then_inc(pT_done, 1)

            def values(m, c):
                if not exists(m, c):
                    return
                b = c // C
                wait(pe, plo_done, m, 8, c + 1)
                if c % C == 0:
                    wait(pe, vlo_done, m, 8, 4 * (b + 1))
                wait(pe, out_done, m, 8, c - 1)
                split_product(ps_o[c % 2][:, :],
                              [pT_hi[:, c % 2, n, :] for n in range(C)], [pT_lo[:, c % 2, n, :] for n in range(C)],
                              [v_hi[:, b % 2, n, :] for n in range(C)], [v_lo[:, b % 2, n, :] for n in range(C)]
                              ).then_inc(values_done, 1)

            def step(m, c):
                scores(m, c)
                transpose_probabilities(m, c - LAG_PT)
                values(m, c - LAG_O)

            pe.wait_ge(onehot_ready, 1)
            for r in range(R):
                last = pe.matmul(ps_bias[:, r * B:(r + 1) * B], embed_sb[:, r, :, :], onehot[:, :],
                                 start=True, stop=True)
            last.then_inc(bias_in_psum, 1)
            pe.wait_ge(ident_ready, 2)
            run_steps(pe, step)


def kernel(**inputs):
    import concourse.bacc as bacc
    from concourse.bass_utils import run_bass_kernel_spmd

    nc = bacc.Bacc("TRN2", target_bir_lowering=False, num_devices=1)
    names = ["x", "fside_BxSxS_0", "itok_B_0_5", "L0_cond_braak_embed"]
    arrays = {f"in_{n}": np.ascontiguousarray(inputs[n]) for n in names}
    args = [nc.dram_tensor(n, a.shape, mybir.dt.from_np(a.dtype), kind="ExternalInput").ap()
            for n, a in arrays.items()]
    out = nc.dram_tensor("out", arrays["in_x"].shape, F32, kind="ExternalOutput").ap()
    attention(nc, *args, out)
    result = run_bass_kernel_spmd(nc, [arrays], core_ids=[0])
    return result.results[0]["out"]
```

```python
import numpy as np

import concourse.bass as bass
from concourse import mybir
from concourse.alu_op_type import AluOpType as ALU

F32 = mybir.dt.float32
F32R = mybir.dt.float32r
I32 = mybir.dt.int32
ACT = mybir.ActivationFunctionType
AX = mybir.AxisListType

P = 128
Q = 32
QUADRANTS = (0, 2, 1, 3)
LEAD_K = 5
LEAD_Q = 2
LEAD_X = 3
LEAD_V = 1
LAG_SUM = 1
LAG_PT = 2
LAG_O = 3
UNROLL = 8
FIRST = 11


def attention(nc, x, f, stage, embed, out):
    B, S, D = x.shape
    C = S // P
    R = S // Q
    N = B * C
    STAGES = embed.shape[0]
    assert S == D == C * P and C == 4 and N % UNROLL == 0
    assert LEAD_K - LEAD_Q >= C - 1 and LEAD_V + LAG_PT >= C - 1
    ROUNDS = (N - LEAD_K - FIRST + 1) // UNROLL
    LAST = N - 1 + LAG_O

    x_rows = x.rearrange("b (i p) d -> b p i d", p=P)
    out_rows = out.rearrange("b (i p) d -> b p i d", p=P)
    v_rows = f.rearrange("b (c p) d -> b p c d", p=P)
    x_blocks = x.rearrange("b (r t) (a n) -> b a t r n", t=Q, a=C)
    f_blocks = f.rearrange("b (r t) (a n) -> b a t r n", t=Q, a=C)

    def sb(name, shape, dt=F32):
        return nc.alloc_sbuf_tensor(name, shape, dt)

    x_sb = sb("x_sb", [P, 2 * C, D])
    v_sb = sb("v_sb", [P, 2, C, D])
    xb_sb = sb("xb_sb", [P, 2, R, P])
    kb_sb = sb("kb_sb", [P, 2, R, P])
    qT_hi = sb("qT_hi", [P, 4, C, P], F32R)
    qT_lo = sb("qT_lo", [P, 4, C, P], F32R)
    kT_hi = sb("kT_hi", [P, 2, C, S], F32R)
    kT_lo = sb("kT_lo", [P, 2, C, S], F32R)
    v_hi = sb("v_hi", [P, 2, C, D], F32R)
    v_lo = sb("v_lo", [P, 2, C, D], F32R)
    p_sb = sb("p_sb", [P, 2, S])
    pb_sb = sb("pb_sb", [P, 4, C, P])
    pT_hi = sb("pT_hi", [P, 2, C, P], F32R)
    pT_lo = sb("pT_lo", [P, 2, C, P], F32R)
    negmax = sb("negmax", [P, 4])
    rowsum = sb("rowsum", [P, 4])
    rowinv = sb("rowinv", [P, 8])
    o_sb = sb("o_sb", [P, 4, D])
    bias = sb("bias", [P, R, B])
    embed_sb = sb("embed_sb", [STAGES, S])
    stage_i = sb("stage_i", [STAGES, C, B], I32)
    stage_f = sb("stage_f", [STAGES, C * B])
    wrap = sb("wrap", [STAGES, C * B])
    onehot = sb("onehot", [STAGES, C * B])
    own_i = sb("own_i", [STAGES, 1], I32)
    own_f = sb("own_f", [STAGES, 1])

    ps_s = [nc.alloc_psum_tensor(f"ps_s{n}", [P, S], F32) for n in range(2)]
    ps_o = [nc.alloc_psum_tensor(f"ps_o{n}", [P, D], F32) for n in range(2)]
    ps_pT = nc.alloc_psum_tensor("ps_pT", [P, C, P], F32)
    ps_q = nc.alloc_psum_tensor("ps_q", [P, C, P], F32)
    ps_k = [nc.alloc_psum_tensor(f"ps_k{n}", [P, S], F32) for n in range(2)]
    ps_bias = ps_o[0]

    sem = nc.alloc_semaphore
    table_loaded = sem("table_loaded")
    own_ready = sem("own_ready")
    setup_step = sem("setup_step")
    onehot_ready = sem("onehot_ready")
    bias_in_psum = sem("bias_in_psum")
    bias_ready = sem("bias_ready")
    x_loaded = [sem(f"x_loaded{n}") for n in range(4)]
    v_loaded = [sem(f"v_loaded{n}") for n in range(2)]
    xb_loaded = [sem(f"xb_loaded{n}") for n in range(2)]
    kb_loaded = [sem(f"kb_loaded{n}") for n in range(2)]
    q_ready = sem("q_ready")
    qT_done = sem("qT_done")
    qhi_done = sem("qhi_done")
    qlo_done = sem("qlo_done")
    kT_done = sem("kT_done")
    khi_done = sem("khi_done")
    klo_done = sem("klo_done")
    vhi_done = sem("vhi_done")
    vlo_done = sem("vlo_done")
    scores_done = sem("scores_done")
    max_done = sem("max_done")
    exp_done = sem("exp_done")
    moved = [sem(f"moved{n}") for n in range(4)]
    pT_done = sem("pT_done")
    phi_done = sem("phi_done")
    plo_done = sem("plo_done")
    inv_done = sem("inv_done")
    values_done = sem("values_done")
    scaled_done = sem("scaled_done")
    out_done = sem("out_done")
    stored = [sem(f"stored{n}") for n in range(2)]

    def wait(eng, s, m, per_round, c):
        if isinstance(m, int):
            if per_round * m + c > 0:
                eng.wait_ge(s, per_round * m + c)
        else:
            assert c > 0, "a wait in a loop starts at zero or below"
            eng.wait_ge(s, m * per_round + c)

    def exists(m, c):
        return 0 <= UNROLL * m + c < N if isinstance(m, int) else True

    def run_steps(eng, step, rounds=ROUNDS, last=LAST):
        for c in range(FIRST):
            step(0, c)
        with eng.Fori(0, rounds) as m:
            for c in range(FIRST, FIRST + UNROLL):
                step(m, c)
        for c in range(FIRST, last + 1 - UNROLL * rounds):
            step(rounds, c)

    with nc.Block() as block:

        @block.sync
        def _(sp):
            def load_x(m, j):
                b, half, slot = 2 * m + j // 2, j % 2, j % 4
                sp.dma_start(x_sb[:, 2 * slot:2 * slot + 2, :], x_rows[b, :, 2 * half:2 * half + 2, :]
                             ).then_inc(x_loaded[slot], 16)

            def load_x_blocks(m, b):
                for a in QUADRANTS:
                    sp.dma_start(xb_sb[Q * a:Q * a + Q, b % 2, :, :], x_blocks[2 * m + b, a, :, :, :]
                                 ).then_inc(xb_loaded[b % 2], 16)

            def load_values(m, b):
                sp.dma_start(v_sb[:, b % 2, :, :], v_rows[2 * m + b, :, :, :]).then_inc(v_loaded[b % 2], 16)

            def load_key_blocks(m, b, quadrants=QUADRANTS):
                for a in quadrants:
                    sp.dma_start(kb_sb[Q * a:Q * a + Q, b % 2, :, :], f_blocks[2 * m + b, a, :, :, :]
                                 ).then_inc(kb_loaded[b % 2], 16)

            def store(m, j):
                half = j % 2
                sp.dma_start(out_rows[2 * m + j // 2, :, 2 * half:2 * half + 2, :],
                             o_sb[:, 2 * half:2 * half + 2, :]).then_inc(stored[half], 16)

            def move_probabilities(m, c):
                for a in QUADRANTS:
                    sp.dma_start(pb_sb[Q * a:Q * a + Q, c % 4, :, :], p_sb[:, c % 2, P * a:P * a + P]
                                 ).then_inc(moved[c % 4], 16)

            def count(m, c):
                value = m * UNROLL + c
                if not isinstance(m, int):
                    sp.compute_val(value)
                return value

            def reach(s, n):
                if not isinstance(n, int) or n > 0:
                    sp.wait_ge(s, n)

            def step(m, c):
                b, phase = c // C, c % C
                moves, loads = exists(m, c), exists(m, c + 2 * C)
                j = 2 * b + phase // 2
                stores = phase % 2 == 1 and exists(m, 2 * j - 4)
                all_of_batch, pair_done = count(m, 4 * b + 4), count(m, 2 * j - 2)
                slot_transposed, tile_done = count(m, c - 3), count(m, c + 1)
                if phase == 0 and loads:
                    reach(kT_done, all_of_batch)
                if phase == 2 and loads:
                    reach(qT_done, all_of_batch)
                if phase == 3 and loads:
                    reach(vlo_done, all_of_batch)
                if stores:
                    reach(out_done, pair_done)
                if moves:
                    reach(pT_done, slot_transposed)
                    reach(exp_done, tile_done)
                    move_probabilities(m, c)
                if phase == 0 and loads:
                    load_key_blocks(m, b + 2)
                if phase == 2 and loads:
                    load_x_blocks(m, b + 2)
                if phase == 3 and loads:
                    load_values(m, b + 2)
                if stores:
                    store(m, j - 2)
                if phase % 2 == 1 and exists(m, 2 * j + 4):
                    load_x(m, j + 2)

            load_key_blocks(0, 0, QUADRANTS[:1])
            sp.dma_start(stage_i[:, :, :], stage.rearrange("(n a b) -> n a b", n=1, a=1).broadcast_to([STAGES, C, B])
                         ).then_inc(table_loaded, 16)
            sp.dma_start(embed_sb[:, :], embed).then_inc(table_loaded, 16)
            load_key_blocks(0, 0, QUADRANTS[1:])
            load_x_blocks(0, 0)
            load_key_blocks(0, 1)
            load_values(0, 0)
            load_x_blocks(0, 1)
            load_x(0, 0)
            load_x(0, 1)
            load_values(0, 1)
            run_steps(sp, step, rounds=ROUNDS - 1, last=N + 3)
            for half in range(2):
                sp.wait_ge(stored[half], 16 * B)

        @block.gpsimd
        def _(pool):
            pool.iota(own_i[:, :], pattern=[[0, 1]], base=0, channel_multiplier=1).then_inc(own_ready, 1)

            def split_values(m, c):
                if not exists(m, c):
                    return
                half, j = c // C % 2, c % C
                wait(pool, vhi_done, m, 8, c + 1)
                pool.tensor_tensor(v_lo[:, half, j, :], v_sb[:, half, j, :], v_hi[:, half, j, :].bitcast(F32),
                                   ALU.subtract).then_inc(vlo_done, 1)

            def add_bias(m, c):
                if not exists(m, c):
                    return
                if c % C == 0:
                    wait(pool, xb_loaded[c // C % 2], m, 64, 64 * (c // 8 + 1))
                half, rows = c // C % 2, slice(c % C * C, c % C * C + C)
                tile = xb_sb[:, half, rows, :]
                pool.tensor_tensor(tile, tile, bias[:, rows, bass.ds(2 * m + c // C, 1)].to_broadcast([P, C, P]),
                                   ALU.add).then_inc(q_ready, 1)

            def result(m, c):
                if not exists(m, c):
                    return
                if c % 2 == 0:
                    wait(pool, x_loaded[c // 2 % 4], m, 16, 16 * (c // 8 + 1))
                wait(pool, scaled_done, m, 8, c + 1)
                pool.tensor_tensor(o_sb[:, c % 4, :], o_sb[:, c % 4, :], x_sb[:, c % 8, :], ALU.add
                                   ).then_inc(out_done, 1)

            def step(m, c):
                add_bias(m, c + LEAD_X)
                split_values(m, c + LEAD_V)
                result(m, c - LAG_O)

            pool.wait_ge(bias_ready, 1)
            for c in range(LEAD_X):
                add_bias(0, c)
            for c in range(LEAD_V):
                split_values(0, c)
            run_steps(pool, step)

        @block.scalar
        def _(act):
            def high_queries(m, c):
                if not exists(m, c):
                    return
                wait(act, qT_done, m, 8, c + 1)
                wait(act, scores_done, m, 8, c - 3)
                act.activation(qT_hi[:, c % 4, :, :], ps_q[:, :, :], ACT.Copy).then_inc(qhi_done, 1)

            def high_keys(m, c):
                if not exists(m, c):
                    return
                b, j = c // C, c % C
                wait(act, kT_done, m, 8, c + 1)
                if j == 0:
                    wait(act, scores_done, m, 8, 4 * (b - 1))
                act.activation(kT_hi[:, b % 2, j, :], ps_k[c % 2][:, :], ACT.Copy).then_inc(khi_done, 1)

            def high_values(m, c):
                if not exists(m, c):
                    return
                b, j = c // C, c % C
                if j == 0:
                    wait(act, v_loaded[b % 2], m, 16, 16 * (b // 2 + 1))
                    wait(act, values_done, m, 8, 4 * (b - 1))
                act.activation(v_hi[:, b % 2, j, :], v_sb[:, b % 2, j, :], ACT.Copy).then_inc(vhi_done, 1)

            def high_probabilities(m, c):
                if not exists(m, c):
                    return
                wait(act, pT_done, m, 8, c + 1)
                wait(act, values_done, m, 8, c - 1)
                act.activation(pT_hi[:, c % 2, :, :], ps_pT[:, :, :], ACT.Copy).then_inc(phi_done, 1)

            def exponentials(m, c):
                if not exists(m, c):
                    return
                wait(act, max_done, m, 8, c + 1)
                wait(act, moved[(c - 2) % 4], m, 128, 64 * ((c - 2) // 4 + 1))
                wait(act, inv_done, m, 8, c - 3)
                act.activation(p_sb[:, c % 2, :], ps_s[c % 2][:, :], ACT.Exp, bias=negmax[:, c % 4:c % 4 + 1],
                               accum_out=rowsum[:, c % 4:c % 4 + 1]).then_inc(exp_done, 1)

            def scale(m, c):
                if not exists(m, c):
                    return
                wait(act, values_done, m, 8, c + 1)
                wait(act, inv_done, m, 8, c + 1)
                if c % 2 == 0:
                    wait(act, stored[c // 2 % 2], m, 32, 16 * (c // 4))
                act.activation(o_sb[:, c % 4, :], ps_o[c % 2][:, :], ACT.Copy, scale=rowinv[:, c % 8:c % 8 + 1]
                               ).then_inc(scaled_done, 1)

            def step(m, c):
                exponentials(m, c)
                high_keys(m, c + LEAD_K)
                high_queries(m, c + LEAD_Q)
                high_values(m, c + LEAD_V)
                high_probabilities(m, c - LAG_PT)
                scale(m, c - LAG_O)

            for c in range(3):
                high_keys(0, c)
            high_queries(0, 0)
            high_keys(0, 3)
            high_queries(0, 1)
            high_keys(0, 4)
            for c in range(LEAD_V):
                high_values(0, c)
            run_steps(act, step)

        @block.vector
        def _(dve):
            dve.wait_ge(table_loaded, 32)
            dve.tensor_copy(stage_f[:, :], stage_i[:, :, :]).then_inc(setup_step, 1)
            dve.wait_ge(own_ready, 1)
            dve.tensor_copy(own_f[:, :], own_i[:, :]).then_inc(setup_step, 1)
            dve.wait_ge(setup_step, 2)
            dve.tensor_scalar(wrap[:, :], stage_f[:, :], 0.0, float(STAGES), ALU.is_lt, ALU.mult
                              ).then_inc(setup_step, 1)
            dve.wait_ge(setup_step, 3)
            dve.tensor_tensor(stage_f[:, :], stage_f[:, :], wrap[:, :], ALU.add).then_inc(setup_step, 1)
            dve.wait_ge(setup_step, 4)
            dve.tensor_scalar(wrap[:, :], stage_f[:, :], 0.0, float(STAGES - 1), ALU.max, ALU.min
                              ).then_inc(setup_step, 1)
            dve.wait_ge(setup_step, 5)
            dve.tensor_scalar(onehot[:, :], wrap[:, :], own_f[:, 0:1], None, ALU.is_equal
                              ).then_inc(onehot_ready, 1)

            def transpose_keys(m, c):
                if not exists(m, c):
                    return
                b, j = c // C, c % C
                if j == 0:
                    wait(dve, kb_loaded[b % 2], m, 64, 64 * (b // 2 + 1))
                wait(dve, klo_done, m, 8, c - 1)
                dve.transpose(ps_k[c % 2][:, :].rearrange("p (a c t) -> p a c t", a=C, c=C),
                              kb_sb[:, b % 2, :, Q * j:Q * j + Q].rearrange("p (c a) t -> p a c t", a=C)
                              ).then_inc(kT_done, 1)

            def transpose_queries(m, c):
                if not exists(m, c):
                    return
                wait(dve, q_ready, m, 8, c + 1)
                wait(dve, qlo_done, m, 8, c)
                rows = slice(c % C * C, c % C * C + C)
                dve.transpose(ps_q[:, :, :].rearrange("p c (r s) -> p r c s", s=Q),
                              xb_sb[:, c // C % 2, rows, :].rearrange("p r (c u) -> p r c u", u=Q)
                              ).then_inc(qT_done, 1)

            def low(m, c, dst, src, hi, done, hi_done):
                wait(dve, hi_done, m, 8, c + 1)
                dve.tensor_tensor(dst, src, hi.bitcast(F32), ALU.subtract).then_inc(done, 1)

            def low_queries(m, c):
                if exists(m, c):
                    low(m, c, qT_lo[:, c % 4, :, :], ps_q[:, :, :], qT_hi[:, c % 4, :, :], qlo_done, qhi_done)

            def low_keys(m, c):
                if exists(m, c):
                    b, j = c // C % 2, c % C
                    low(m, c, kT_lo[:, b, j, :], ps_k[c % 2][:, :], kT_hi[:, b, j, :], klo_done, khi_done)

            def low_probabilities(m, c):
                if exists(m, c):
                    low(m, c, pT_lo[:, c % 2, :, :], ps_pT[:, :, :], pT_hi[:, c % 2, :, :], plo_done, phi_done)

            def maximum(m, c):
                if not exists(m, c):
                    return
                wait(dve, scores_done, m, 8, c + 1)
                wait(dve, exp_done, m, 8, c - 3)
                dve.reduce_max(negmax[:, c % 4:c % 4 + 1], ps_s[c % 2][:, :], axis=AX.X, negate=True
                               ).then_inc(max_done, 1)

            def inverse(m, c):
                if not exists(m, c):
                    return
                wait(dve, exp_done, m, 8, c + 1)
                wait(dve, scaled_done, m, 8, c - 7)
                dve.reciprocal(rowinv[:, c % 8:c % 8 + 1], rowsum[:, c % 4:c % 4 + 1]).then_inc(inv_done, 1)

            def transpose_probabilities(m, c):
                if not exists(m, c):
                    return
                wait(dve, moved[c % 4], m, 128, 64 * (c // 4 + 1))
                wait(dve, plo_done, m, 8, c)
                dve.transpose(ps_pT[:, :, :].rearrange("p c (j r) -> p r c j", r=C),
                              pb_sb[:, c % 4, :, :].rearrange("p r (c u) -> p r c u", u=Q)).then_inc(pT_done, 1)

            def step(m, c):
                maximum(m, c)
                transpose_keys(m, c + LEAD_K)
                transpose_queries(m, c + LEAD_Q)
                transpose_probabilities(m, c - LAG_PT)
                low_keys(m, c + LEAD_K)
                low_queries(m, c + LEAD_Q)
                low_probabilities(m, c - LAG_PT)
                inverse(m, c - LAG_SUM)

            transpose_keys(0, 0)
            transpose_keys(0, 1)
            low_keys(0, 0)
            dve.wait_ge(bias_in_psum, 1)
            dve.transpose(bias[:, :, :], ps_bias[:, :]).then_inc(bias_ready, 1)
            transpose_keys(0, 2)
            low_keys(0, 1)
            transpose_queries(0, 0)
            transpose_keys(0, 3)
            low_queries(0, 0)
            low_keys(0, 2)
            transpose_queries(0, 1)
            low_keys(0, 3)
            low_queries(0, 1)
            transpose_keys(0, 4)
            low_keys(0, 4)
            run_steps(dve, step)

        @block.tensor
        def _(pe):
            def split_product(bank, lhs_hi, lhs_lo, rhs_hi, rhs_lo, before):
                terms = [t for n in range(C) for t in
                         ((lhs_lo[n], rhs_hi[n]), (lhs_hi[n], rhs_lo[n]), (lhs_hi[n], rhs_hi[n]))]
                for n, (lhs, rhs) in enumerate(terms):
                    before(n)
                    last = pe.matmul(bank, lhs, rhs, start=(n == 0), stop=(n == len(terms) - 1))
                return last

            def scores(m, c):
                if not exists(m, c):
                    return
                b = c // C
                wait(pe, qlo_done, m, 8, c + 1)

                def before(n):
                    if isinstance(m, int) and UNROLL * m + c == 0 and n % 3 == 0:
                        pe.wait_ge(klo_done, n // 3 + 1)

                wait(pe, exp_done, m, 8, c - 1)
                split_product(ps_s[c % 2][:, :],
                              [qT_hi[:, c % 4, n, :] for n in range(C)], [qT_lo[:, c % 4, n, :] for n in range(C)],
                              [kT_hi[:, b % 2, n, :] for n in range(C)], [kT_lo[:, b % 2, n, :] for n in range(C)],
                              before).then_inc(scores_done, 1)

            def values(m, c):
                if not exists(m, c):
                    return
                b = c // C
                wait(pe, plo_done, m, 8, c + 1)

                def before(n):
                    if c % C == 0 and n == 1:
                        wait(pe, vlo_done, m, 8, 4 * (b + 1))

                wait(pe, scaled_done, m, 8, c - 1)
                split_product(ps_o[c % 2][:, :],
                              [pT_hi[:, c % 2, n, :] for n in range(C)], [pT_lo[:, c % 2, n, :] for n in range(C)],
                              [v_hi[:, b % 2, n, :] for n in range(C)], [v_lo[:, b % 2, n, :] for n in range(C)],
                              before
                              ).then_inc(values_done, 1)

            def step(m, c):
                scores(m, c)
                values(m, c - LAG_O)

            pe.wait_ge(onehot_ready, 1)
            pe.matmul(ps_bias[:, :], onehot[:, :], embed_sb[:, :], start=True, stop=True).then_inc(bias_in_psum, 1)
            run_steps(pe, step)


def kernel(**inputs):
    import concourse.bacc as bacc
    from concourse.bass_utils import run_bass_kernel_spmd

    nc = bacc.Bacc("TRN2", target_bir_lowering=False, num_devices=1)
    names = ["x", "fside_BxSxS_0", "itok_B_0_5", "L0_cond_braak_embed"]
    arrays = {f"in_{n}": np.ascontiguousarray(inputs[n]) for n in names}
    args = [nc.dram_tensor(n, a.shape, mybir.dt.from_np(a.dtype), kind="ExternalInput").ap()
            for n, a in arrays.items()]
    out = nc.dram_tensor("out", arrays["in_x"].shape, F32, kind="ExternalOutput").ap()
    attention(nc, *args, out)
    result = run_bass_kernel_spmd(nc, [arrays], core_ids=[0])
    return result.results[0]["out"]
```
